# Optimizing a Trainium2 kernel written in Bass

```python
import numpy as np
import jax
import jax.numpy as jnp

def _softmax(x, axis=-1):
    return jax.nn.softmax(x, axis=axis)

def _gelu(x):
    return jax.nn.gelu(x, approximate=True)

def _silu(x):
    return jax.nn.silu(x)

def _sigmoid(x):
    return jax.nn.sigmoid(x)

def _layernorm(x, axis=-1, eps=1e-05):
    m = jnp.mean(x, axis=axis, keepdims=True)
    v = jnp.var(x, axis=axis, keepdims=True)
    return (x - m) / jnp.sqrt(v + eps)

def _scatter_add(tgt, idx, src, axis=0):
    return tgt.at[idx].add(src)

def _segment_sum(src, seg, n):
    return jax.ops.segment_sum(src, seg, n)
kernel_name = 'mk_dlrm_tower_d1_rec_r8_91e5a3'

def setup_inputs(seed: int=0):
    np.random.seed(seed)
    _w = jnp.asarray

    def _rec_inputs():
        import jax
        import jax.numpy as jnp
        _tk = jax.random.key(seed)
        ids = jnp.stack([jax.random.randint(jax.random.fold_in(_tk, 200 + f), (512,), 0, v, jnp.int32) for f, v in enumerate([1000, 125000, 12500, 12500, 1250, 12500, 1000, 12500, 1000, 12500, 1250, 12500, 1250, 1250, 12500, 1000, 1250, 1250, 1000, 12500, 1000, 1250, 1250, 1250, 1250, 1250, 1000])], axis=1)
        tbl_0 = 0.05 * jax.random.normal(jax.random.fold_in(_tk, 500 + 0), (1000, 128), jnp.float32)
        tbl_1 = 0.05 * jax.random.normal(jax.random.fold_in(_tk, 500 + 1), (125000, 128), jnp.float32)
        tbl_2 = 0.05 * jax.random.normal(jax.random.fold_in(_tk, 500 + 2), (12500, 128), jnp.float32)
        tbl_3 = 0.05 * jax.random.normal(jax.random.fold_in(_tk, 500 + 3), (12500, 128), jnp.float32)
        tbl_4 = 0.05 * jax.random.normal(jax.random.fold_in(_tk, 500 + 4), (1250, 128), jnp.float32)
        tbl_5 = 0.05 * jax.random.normal(jax.random.fold_in(_tk, 500 + 5), (12500, 128), jnp.float32)
        tbl_6 = 0.05 * jax.random.normal(jax.random.fold_in(_tk, 500 + 6), (1000, 128), jnp.float32)
        tbl_7 = 0.05 * jax.random.normal(jax.random.fold_in(_tk, 500 + 7), (12500, 128), jnp.float32)
        tbl_8 = 0.05 * jax.random.normal(jax.random.fold_in(_tk, 500 + 8), (1000, 128), jnp.float32)
        tbl_9 = 0.05 * jax.random.normal(jax.random.fold_in(_tk, 500 + 9), (12500, 128), jnp.float32)
        tbl_10 = 0.05 * jax.random.normal(jax.random.fold_in(_tk, 500 + 10), (1250, 128), jnp.float32)
        tbl_11 = 0.05 * jax.random.normal(jax.random.fold_in(_tk, 500 + 11), (12500, 128), jnp.float32)
        tbl_12 = 0.05 * jax.random.normal(jax.random.fold_in(_tk, 500 + 12), (1250, 128), jnp.float32)
        tbl_13 = 0.05 * jax.random.normal(jax.random.fold_in(_tk, 500 + 13), (1250, 128), jnp.float32)
        tbl_14 = 0.05 * jax.random.normal(jax.random.fold_in(_tk, 500 + 14), (12500, 128), jnp.float32)
        tbl_15 = 0.05 * jax.random.normal(jax.random.fold_in(_tk, 500 + 15), (1000, 128), jnp.float32)
        tbl_16 = 0.05 * jax.random.normal(jax.random.fold_in(_tk, 500 + 16), (1250, 128), jnp.float32)
        tbl_17 = 0.05 * jax.random.normal(jax.random.fold_in(_tk, 500 + 17), (1250, 128), jnp.float32)
        tbl_18 = 0.05 * jax.random.normal(jax.random.fold_in(_tk, 500 + 18), (1000, 128), jnp.float32)
        tbl_19 = 0.05 * jax.random.normal(jax.random.fold_in(_tk, 500 + 19), (12500, 128), jnp.float32)
        tbl_20 = 0.05 * jax.random.normal(jax.random.fold_in(_tk, 500 + 20), (1000, 128), jnp.float32)
        tbl_21 = 0.05 * jax.random.normal(jax.random.fold_in(_tk, 500 + 21), (1250, 128), jnp.float32)
        tbl_22 = 0.05 * jax.random.normal(jax.random.fold_in(_tk, 500 + 22), (1250, 128), jnp.float32)
        tbl_23 = 0.05 * jax.random.normal(jax.random.fold_in(_tk, 500 + 23), (1250, 128), jnp.float32)
        tbl_24 = 0.05 * jax.random.normal(jax.random.fold_in(_tk, 500 + 24), (1250, 128), jnp.float32)
        tbl_25 = 0.05 * jax.random.normal(jax.random.fold_in(_tk, 500 + 25), (1250, 128), jnp.float32)
        tbl_26 = 0.05 * jax.random.normal(jax.random.fold_in(_tk, 500 + 26), (1000, 128), jnp.float32)
        _rk = jax.random.fold_in(_tk, 7)
        r_bottom_mlp_out = 4.13588e-05 + 0.999923 * jax.random.normal(jax.random.fold_in(_rk, 101), (512, 128), jnp.float32)
        W_top1 = 0.0405887 * jax.random.normal(jax.random.fold_in(_tk, 801), (607, 512), jnp.float32)
        W_top2 = 0.0441942 * jax.random.normal(jax.random.fold_in(_tk, 802), (512, 256), jnp.float32)
        W_top3 = 0.0625 * jax.random.normal(jax.random.fold_in(_tk, 803), (256, 1), jnp.float32)
        b_top1 = jnp.zeros((512,), jnp.float32)
        b_top2 = jnp.zeros((256,), jnp.float32)
        return (r_bottom_mlp_out, ids, tbl_0, tbl_1, tbl_2, tbl_3, tbl_4, tbl_5, tbl_6, tbl_7, tbl_8, tbl_9, tbl_10, tbl_11, tbl_12, tbl_13, tbl_14, tbl_15, tbl_16, tbl_17, tbl_18, tbl_19, tbl_20, tbl_21, tbl_22, tbl_23, tbl_24, tbl_25, tbl_26, W_top1, b_top1, W_top2, b_top2, W_top3)
    r_bottom_mlp_out, ids, tbl_0, tbl_1, tbl_2, tbl_3, tbl_4, tbl_5, tbl_6, tbl_7, tbl_8, tbl_9, tbl_10, tbl_11, tbl_12, tbl_13, tbl_14, tbl_15, tbl_16, tbl_17, tbl_18, tbl_19, tbl_20, tbl_21, tbl_22, tbl_23, tbl_24, tbl_25, tbl_26, W_top1, b_top1, W_top2, b_top2, W_top3 = _rec_inputs()

    def _L0_rec_setup():
        import jax, jax.numpy as jnp
        import numpy as np
        NUM_FEATURES = 27

        def _tril_indices(F):
            idx = []
            for i in range(F):
                for j in range(i):
                    idx.append(i * F + j)
            return np.asarray(idx, dtype=np.int32)
        TRIL_IDX = _tril_indices(NUM_FEATURES)
        key = jax.random.key(seed)
        k1, k2 = jax.random.split(key)
        B, F, D = (8192, NUM_FEATURES, 128)
        features = jax.random.normal(k1, (B, F, D), dtype=jnp.float32)
        bottom_mlp_out = jax.random.normal(k2, (B, D), dtype=jnp.float32)
        return {'features': features, 'bottom_mlp_out': bottom_mlp_out}
    _L0_rec_all = _L0_rec_setup()
    _L0_rec_in = {k: v for k, v in _L0_rec_all.items() if k in ()}
    del _L0_rec_all
    return {'r_bottom_mlp_out': r_bottom_mlp_out, 'ids': ids, 'tbl_0': tbl_0, 'tbl_1': tbl_1, 'tbl_2': tbl_2, 'tbl_3': tbl_3, 'tbl_4': tbl_4, 'tbl_5': tbl_5, 'tbl_6': tbl_6, 'tbl_7': tbl_7, 'tbl_8': tbl_8, 'tbl_9': tbl_9, 'tbl_10': tbl_10, 'tbl_11': tbl_11, 'tbl_12': tbl_12, 'tbl_13': tbl_13, 'tbl_14': tbl_14, 'tbl_15': tbl_15, 'tbl_16': tbl_16, 'tbl_17': tbl_17, 'tbl_18': tbl_18, 'tbl_19': tbl_19, 'tbl_20': tbl_20, 'tbl_21': tbl_21, 'tbl_22': tbl_22, 'tbl_23': tbl_23, 'tbl_24': tbl_24, 'tbl_25': tbl_25, 'tbl_26': tbl_26, 'W_top1': W_top1, 'b_top1': b_top1, 'W_top2': W_top2, 'b_top2': b_top2, 'W_top3': W_top3}

def reference(r_bottom_mlp_out, ids, tbl_0, tbl_1, tbl_2, tbl_3, tbl_4, tbl_5, tbl_6, tbl_7, tbl_8, tbl_9, tbl_10, tbl_11, tbl_12, tbl_13, tbl_14, tbl_15, tbl_16, tbl_17, tbl_18, tbl_19, tbl_20, tbl_21, tbl_22, tbl_23, tbl_24, tbl_25, tbl_26, W_top1, b_top1, W_top2, b_top2, W_top3):
    import jax
    import jax.numpy as jnp

    def _L0_rec_ref(features, bottom_mlp_out):
        import jax, jax.numpy as jnp
        import numpy as np
        NUM_FEATURES = 27

        def _tril_indices(F):
            idx = []
            for i in range(F):
                for j in range(i):
                    idx.append(i * F + j)
            return np.asarray(idx, dtype=np.int32)
        TRIL_IDX = _tril_indices(NUM_FEATURES)
        B = features.shape[0]
        F = features.shape[1]
        interactions = jnp.einsum('bfd,bgd->bfg', features, features)
        interactions = interactions.reshape(B, F * F)
        x = interactions[:, TRIL_IDX]
        return jnp.concatenate([bottom_mlp_out, x], axis=1)
    e = jnp.stack([tbl_0[ids[:, 0]], tbl_1[ids[:, 1]], tbl_2[ids[:, 2]], tbl_3[ids[:, 3]], tbl_4[ids[:, 4]], tbl_5[ids[:, 5]], tbl_6[ids[:, 6]], tbl_7[ids[:, 7]], tbl_8[ids[:, 8]], tbl_9[ids[:, 9]], tbl_10[ids[:, 10]], tbl_11[ids[:, 11]], tbl_12[ids[:, 12]], tbl_13[ids[:, 13]], tbl_14[ids[:, 14]], tbl_15[ids[:, 15]], tbl_16[ids[:, 16]], tbl_17[ids[:, 17]], tbl_18[ids[:, 18]], tbl_19[ids[:, 19]], tbl_20[ids[:, 20]], tbl_21[ids[:, 21]], tbl_22[ids[:, 22]], tbl_23[ids[:, 23]], tbl_24[ids[:, 24]], tbl_25[ids[:, 25]], tbl_26[ids[:, 26]]], axis=1)
    z = _L0_rec_ref(e, r_bottom_mlp_out)
    z = z.reshape(z.shape[0], -1)
    h = jnp.concatenate([z, r_bottom_mlp_out], axis=1)
    h = jnp.maximum(h @ W_top1 + b_top1, 0.0)
    h = jnp.maximum(h @ W_top2 + b_top2, 0.0)
    y = h @ W_top3
    return y

_drawn_inputs = setup_inputs


def setup_inputs(seed=0):
    import zlib

    import numpy as np

    out = dict(_drawn_inputs(seed))
    spreads = {'b_top1': (0.0, 0.1), 'b_top2': (0.0, 0.1)}
    factors = {'tbl_0': 4.758,
     'tbl_1': 4.876,
     'tbl_2': 4.249,
     'tbl_3': 4.067,
     'tbl_4': 4.84,
     'tbl_5': 4.098,
     'tbl_6': 4.617,
     'tbl_7': 3.988,
     'tbl_8': 4.215,
     'tbl_9': 4.803,
     'tbl_10': 4.18,
     'tbl_11': 4.52,
     'tbl_12': 4.231,
     'tbl_13': 4.524,
     'tbl_14': 4.539,
     'tbl_15': 4.802,
     'tbl_16': 4.649,
     'tbl_17': 4.97,
     'tbl_18': 4.269,
     'tbl_19': 4.206,
     'tbl_20': 4.381,
     'tbl_21': 4.874,
     'tbl_22': 4.533,
     'tbl_23': 4.879,
     'tbl_24': 4.09,
     'tbl_25': 4.858,
     'tbl_26': 4.303}
    for name, (base, spread) in spreads.items():
        noise = np.random.default_rng([zlib.crc32(name.encode()), seed]).standard_normal(out[name].shape)
        drawn = base * np.exp(spread * noise) if base else spread * noise
        out[name] = jnp.asarray(drawn.astype(out[name].dtype))
    for name, factor in factors.items():
        out[name] = (out[name] * factor).astype(out[name].dtype)
    return out
```

```python
from contextlib import ExitStack

import concourse.bass as bass
from concourse import mybir

F32 = mybir.dt.float32
I32 = mybir.dt.int32
ALU = mybir.AluOpType
ACT = mybir.ActivationFunctionType

P = 128
Q = 32
F = 27
D = 128
PACK = P // Q
NC = (F - 1 + PACK - 1) // PACK


def build_tower(nc, bottom, ids, tables, w_bottom, w_inter, b1, w2, b2, w3, ident_in, out):
    B = bottom.shape[0]
    T = B // P
    N1 = w_inter.shape[2]
    M1 = N1 // P
    N2 = w2.shape[2]
    M2 = N2 // P
    GROUPS = [list(range(f, min(f + 4, F))) for f in range(0, F, 4)]
    NG = len(GROUPS)
    HALF = Q // 2
    with ExitStack() as ctx:
        def sb(name, shape, dt=F32):
            return ctx.enter_context(nc.sbuf_tensor(name, shape, dt))

        def ps(name, shape):
            return ctx.enter_context(nc.psum_tensor(name, shape, F32))

        def sem(name):
            return ctx.enter_context(nc.semaphore(name))

        ids_sb = sb("ids_sb", [P, T, F], I32)
        rows = sb("rows", [P, T, F, D])
        xt = sb("xt", [D, T, P, F])
        bot = sb("bot", [P, T, D])
        bot_t = sb("bot_t", [D, T, P])
        ident = sb("ident", [P, P])
        wb = sb("wb", [P, 2, N1])
        wbs = sb("wbs", [P, N1])
        wi = sb("wi", [P, NC, N1])
        w2_sb = sb("w2_sb", [P, M1, N2])
        w3_sb = sb("w3_sb", [P, M2])
        b1_sb = sb("b1_sb", [P, M1])
        b2_sb = sb("b2_sb", [P, M2])
        z = sb("z", [P, 2, NC, P])
        h1 = sb("h1", [P, 2, M1, P])
        h2 = sb("h2", [P, 2, M2, P])
        y_sb = sb("y_sb", [1, B])

        tp = [ps(f"tp{k}", [P, 4, P]) for k in range(3)]
        gram = ps("gram", [P, 2, 512])
        h1_ps = ps("h1_ps", [P, M1, P])
        h2_ps = ps("h2_ps", [P, 512])
        y_ps = ps("y_ps", [1, 512])

        ids_in = sem("ids_in")
        ident_in_s = sem("ident_in")
        bot_in = sem("bot_in")
        wb_in = sem("wb_in")
        wi_in = sem("wi_in")
        w2_in = sem("w2_in")
        small_in = sem("small_in")
        row_in = [[sem(f"row_in{t}_{g}") for g in range(NG)] for t in range(T)]
        turned = sem("turned")
        tp_copied_v = sem("tp_copied_v")
        tp_copied_s = sem("tp_copied_s")
        wbs_ready = sem("wbs_ready")
        z_zeroed = sem("z_zeroed")
        gram_ready = sem("gram_ready")
        packed_v = sem("packed_v")
        packed_s = sem("packed_s")
        h1_done = sem("h1_done")
        h1_ready = sem("h1_ready")
        h2_done = sem("h2_done")
        h2_ready = sem("h2_ready")
        y_done = sem("y_done")
        y_ready = sem("y_ready")
        out_done = sem("out_done")

        def bank(t, g):
            return 1 + t * NG + g

        def copied_by(n):
            return (tp_copied_v, n // 2 + 1) if n % 2 == 0 else (tp_copied_s, (n + 1) // 2)

        def evacuate(copy, eng, n):
            eng.wait_ge(turned, n + 1)
            if n == 0:
                return copy(bot_t[:, :, :], tp[0][:, 0:T, :])
            t, g = (n - 1) // NG, (n - 1) % NG
            fs = GROUPS[g]
            src = tp[n % 3][:, 0:len(fs), :].rearrange("d f b -> d b f")
            return copy(xt[:, t, :, fs[0]:fs[-1] + 1], src)

        def pack(copy, eng, t, slots):
            eng.wait_ge(gram_ready, t + 1)
            eng.wait_ge(z_zeroed, 1)
            if t >= 2:
                eng.wait_ge(h1_done, t - 1)
            for s in slots:
                for g in range(PACK):
                    n = len(range(g, F - 1, PACK))
                    src = gram[Q * s:Q * s + F, :, 0:HALF * F].rearrange("i h (q j) -> i h q j", j=F)
                    dst = z[Q * g:Q * g + F, t % 2, 0:n, Q * s:Q * s + Q].rearrange("i c (h q) -> i h q c", h=2)
                    last = copy(dst, src[:, :, :, g:g + PACK * (n - 1) + 1:PACK])
            return last

        block = ctx.enter_context(nc.Block())

        @block.sync
        def _(sp):
            sp.dma_start(ids_sb[:, :, :], ids.rearrange("(t p) f -> p t f", p=P)).then_inc(ids_in, 16)
            sp.dma_start(ident[:, :], ident_in).then_inc(ident_in_s, 16)
            sp.dma_start(bot[:, :, :], bottom.rearrange("(t p) d -> p t d", p=P)).then_inc(bot_in, 16)
            sp.dma_start(wb[:, :, :], w_bottom).then_inc(wb_in, 16)
            sp.dma_start(wi[:, :, :], w_inter).then_inc(wi_in, 16)
            sp.dma_start(w2_sb[:, :, :], w2).then_inc(w2_in, 16)
            sp.dma_start(w3_sb[:, :], w3).then_inc(small_in, 16)
            sp.dma_start(b1_sb[:, :], b1).then_inc(small_in, 16)
            sp.dma_start(b2_sb[:, :], b2).then_inc(small_in, 16)
            sp.wait_ge(y_ready, T)
            sp.dma_start(out.rearrange("b o -> o b"), y_sb[:, :]).then_inc(out_done, 16)
            sp.wait_ge(out_done, 16)

        @block.gpsimd
        def _(pool):
            pool.wait_ge(ids_in, 16)
            for t in range(T):
                for g, fs in enumerate(GROUPS):
                    for f in fs:
                        pool.indirect_dma_start(
                            rows[:, t, f, :], None, tables[f],
                            bass.IndirectOffsetOnAxis(ap=ids_sb[:, t, f:f + 1], axis=0),
                        ).then_inc(row_in[t][g], 16)

        @block.tensor
        def _(pe):
            pe.wait_ge(ident_in_s, 16)
            pe.wait_ge(bot_in, 16)
            for t in range(T):
                last = pe.transpose(tp[0][:, t, :], bot[:, t, :], ident[:, :])
            last.then_inc(turned, 1)

            def turn(t):
                for g, fs in enumerate(GROUPS):
                    n = bank(t, g)
                    if n >= 3:
                        pe.wait_ge(*copied_by(n - 3))
                    pe.wait_ge(row_in[t][g], 16 * len(fs))
                    for k, f in enumerate(fs):
                        last = pe.transpose(tp[n % 3][:, k, :], rows[:, t, f, :], ident[:, :])
                    last.then_inc(turned, 1)

            def grams(t):
                pe.wait_ge(*copied_by(bank(t, NG - 1)))
                pe.wait_ge(*copied_by(bank(t, NG - 2)))
                if t >= 1:
                    pe.wait_ge(packed_v, t)
                    pe.wait_ge(packed_s, t)
                for q in range(Q):
                    at = (q % HALF) * F
                    for s in range(PACK):
                        x = xt[:, t, Q * s + q, :]
                        last = pe.matmul(gram[Q * s:Q * s + F, q // HALF, at:at + F], x, x,
                                         start=True, stop=True)
                last.then_inc(gram_ready, 1)

            def mlp(t):
                if t == 0:
                    pe.wait_ge(wbs_ready, 1)
                    pe.wait_ge(wi_in, 16)
                    pe.wait_ge(*copied_by(0))
                else:
                    pe.wait_ge(h1_ready, t)
                pe.wait_ge(packed_v, t + 1)
                pe.wait_ge(packed_s, t + 1)
                for m in range(M1):
                    cols = slice(m * P, (m + 1) * P)
                    pe.matmul(h1_ps[:, m, :], wbs[:, cols], bot_t[:, t, :], start=True, stop=False)
                    for c in range(NC):
                        k = Q * len(range(PACK * c, min(PACK * c + PACK, F - 1)))
                        last = pe.matmul(h1_ps[:, m, :], wi[0:k, c, cols], z[0:k, t % 2, c, :],
                                         start=False, stop=(c == NC - 1))
                last.then_inc(h1_done, 1)
                if t == 0:
                    pe.wait_ge(w2_in, 16)
                    pe.wait_ge(small_in, 48)
                pe.wait_ge(h1_ready, t + 1)
                if t >= 1:
                    pe.wait_ge(h2_ready, t)
                for m in range(M2):
                    for c in range(M1):
                        last = pe.matmul(h2_ps[:, m * P:(m + 1) * P], w2_sb[:, c, m * P:(m + 1) * P],
                                         h1[:, t % 2, c, :], start=(c == 0), stop=(c == M1 - 1))
                last.then_inc(h2_done, 1)
                pe.wait_ge(h2_ready, t + 1)
                if t >= 1:
                    pe.wait_ge(y_ready, t)
                for m in range(M2):
                    last = pe.matmul(y_ps[0:1, 0:P], w3_sb[:, m:m + 1], h2[:, t % 2, m, :],
                                     start=(m == 0), stop=(m == M2 - 1))
                last.then_inc(y_done, 1)

            for t in range(T):
                turn(t)
                if t >= 1:
                    mlp(t - 1)
                grams(t)
            mlp(T - 1)

        @block.vector
        def _(dve):
            dve.memset(z[:, :, :, :], 0.0).then_inc(z_zeroed, 1)
            evacuate(dve.tensor_copy, dve, 0).then_inc(tp_copied_v, 1)
            dve.wait_ge(wb_in, 16)
            dve.tensor_tensor(wbs[:, :], wb[:, 0, :], wb[:, 1, :], ALU.add).then_inc(wbs_ready, 1)

            def head(t):
                dve.wait_ge(h2_done, t + 1)
                if t == 0:
                    dve.wait_ge(small_in, 48)
                if t >= 2:
                    dve.wait_ge(y_done, t - 1)
                for m in range(M2):
                    last = dve.tensor_scalar(h2[:, t % 2, m, :], h2_ps[:, m * P:(m + 1) * P],
                                             b2_sb[:, m:m + 1], 0.0, ALU.add, ALU.max)
                last.then_inc(h2_ready, 1)
                dve.wait_ge(y_done, t + 1)
                dve.tensor_copy(y_sb[0:1, t * P:(t + 1) * P], y_ps[0:1, 0:P]).then_inc(y_ready, 1)

            for t in range(T):
                for g in range(NG):
                    if bank(t, g) % 2 == 0:
                        evacuate(dve.tensor_copy, dve, bank(t, g)).then_inc(tp_copied_v, 1)
                if t >= 1:
                    head(t - 1)
                pack(dve.tensor_copy, dve, t, range(0, PACK // 2)).then_inc(packed_v, 1)
            head(T - 1)

        @block.scalar
        def _(act):
            def hidden(t):
                act.wait_ge(h1_done, t + 1)
                if t == 0:
                    act.wait_ge(small_in, 48)
                if t >= 2:
                    act.wait_ge(h2_done, t - 1)
                for m in range(M1):
                    last = act.activation(h1[:, t % 2, m, :], h1_ps[:, m, :], ACT.Relu, bias=b1_sb[:, m:m + 1])
                last.then_inc(h1_ready, 1)

            for t in range(T):
                for g in range(NG):
                    if bank(t, g) % 2 == 1:
                        evacuate(act.copy, act, bank(t, g)).then_inc(tp_copied_s, 1)
                if t >= 1:
                    hidden(t - 1)
                pack(act.copy, act, t, range(PACK // 2, PACK)).then_inc(packed_s, 1)
            hidden(T - 1)


def kernel(**inputs):
    import numpy as np
    import concourse.bacc as bacc
    from concourse.bass_utils import run_bass_kernel_spmd

    nc = bacc.Bacc("TRN2", target_bir_lowering=False, num_devices=1)
    w1 = np.asarray(inputs["W_top1"])
    n1 = w1.shape[1]
    w_inter = np.zeros((P, NC, n1), w1.dtype)
    for i in range(F):
        for j in range(i):
            w_inter[Q * (j % PACK) + i, j // PACK] = w1[D + i * (i - 1) // 2 + j]
    w_bottom = np.ascontiguousarray(np.stack([w1[:D], w1[-D:]], axis=1))

    def columns(a):
        a = np.asarray(a)
        return np.ascontiguousarray(a.reshape((a.shape[0] // P, P) + a.shape[1:]).swapaxes(0, 1))

    arrays = {
        "bottom": np.asarray(inputs["r_bottom_mlp_out"]), "ids": np.asarray(inputs["ids"]),
        "w_bottom": w_bottom, "w_inter": w_inter, "b1": columns(inputs["b_top1"]),
        "w2": columns(inputs["W_top2"]), "b2": columns(inputs["b_top2"]),
        "w3": columns(np.asarray(inputs["W_top3"])[:, 0]), "ident": np.eye(P, dtype=np.float32),
    }
    for f in range(F):
        arrays[f"tbl_{f}"] = np.asarray(inputs[f"tbl_{f}"])
    ap = {k: nc.dram_tensor(k + "_dram", a.shape, mybir.dt.from_np(a.dtype), kind="ExternalInput").ap() for k, a in arrays.items()}
    out = nc.dram_tensor("y_dram", (arrays["bottom"].shape[0], 1), F32, kind="ExternalOutput").ap()
    build_tower(nc, ap["bottom"], ap["ids"], [ap[f"tbl_{f}"] for f in range(F)], ap["w_bottom"], ap["w_inter"],
                ap["b1"], ap["w2"], ap["b2"], ap["w3"], ap["ident"], out)
    r = run_bass_kernel_spmd(nc, [{k + "_dram": a for k, a in arrays.items()}], core_ids=[0])
    return r.results[0]["y_dram"]
```

```python
from contextlib import ExitStack

import concourse.bass as bass
from concourse import mybir

F32 = mybir.dt.float32
I32 = mybir.dt.int32
ALU = mybir.AluOpType
ACT = mybir.ActivationFunctionType

P = 128
Q = 32
F = 27
D = 128
PACK = P // Q
HF = (F - 1) // 2
SLOTS = HF + 1
NC = (SLOTS + PACK - 1) // PACK
R = 125
MAXC = 10
HOT = 7


def build_tower(nc, bottom, ids, ids_hot, tables, gathered, hot, w_bottom, w_inter, b1, w2, b2, w3, ident_in, hot_row_in, mask_in, out):
    B = bottom.shape[0]
    T = B // P
    N1 = w_inter.shape[2]
    M1 = N1 // P
    N2 = w2.shape[2]
    M2 = N2 // P
    G = len(gathered)
    H = len(hot)
    GROUPS = [list(range(f, min(f + 4, G))) for f in range(0, G, 4)]
    NG = len(GROUPS)
    EARLY = range(0, 3)
    LATE = range(3, NG)
    HALF = Q // 2
    chunks = [tables[f].shape[0] // R for f in hot]
    before = [sum(chunks[:n]) for n in range(H + 1)]
    NOV, NOS = 6, 2
    by_vector = [(n, c) for n in range(H) for c in range(chunks[n]) if c % 4 != 3]
    by_scalar = [(n, c) for n in range(H) for c in range(chunks[n]) if c % 4 == 3]

    def chunk_number(made, j):
        n, c = made[j]
        return before[n] + c

    def made_before(made, n, c=0):
        return sum(m < (n, c) for m in made)

    F32R = mybir.dt.float32r
    with ExitStack() as ctx:
        def sb(name, shape, dt=F32):
            return ctx.enter_context(nc.sbuf_tensor(name, shape, dt))

        def ps(name, shape):
            return ctx.enter_context(nc.psum_tensor(name, shape, F32))

        def sem(name):
            return ctx.enter_context(nc.semaphore(name))

        ids_sb = sb("ids_sb", [P, T, F], I32)
        rows = sb("rows", [P, T, G, D])
        xt = sb("xt", [D, T, P, F])
        bot = sb("bot", [P, T, D])
        bot_t = sb("bot_t", [D, T, P])
        ident = sb("ident", [P, P])
        wb = sb("wb", [P, 2, N1])
        wbs = sb("wbs", [P, N1])
        wi = sb("wi", [P, NC, N1])
        w2_sb = sb("w2_sb", [P, M1, N2])
        w3_sb = sb("w3_sb", [P, M2])
        b1_sb = sb("b1_sb", [P, M1])
        b2_sb = sb("b2_sb", [P, M2])
        z = sb("z", [P, 2, NC, P])
        h1 = sb("h1", [P, 2, M1, P])
        h2 = sb("h2", [P, 2, M2, P])
        y_sb = sb("y_sb", [1, B])
        mask = sb("mask", [P, NC], I32)
        hot_row = sb("hot_row", [P, 2, 2, MAXC])
        ids_i = sb("ids_i", [H, B], I32)
        ids_r = sb("ids_r", [H, B], F32R)
        spread = sb("spread", [H, H, P], F32R)
        tab = sb("tab", [R, 3, MAXC * D])
        tab_hi = sb("tab_hi", [R, 3, MAXC * D], F32R)
        tab_lo = sb("tab_lo", [R, 3, MAXC * D], F32R)
        onehot_v = sb("onehot_v", [R, NOV, B], F32R)
        onehot_s = sb("onehot_s", [R, NOS, B], F32R)
        distance = sb("distance", [R, NOS, B])

        NTP = 2
        HM = M1 // 2
        tp = [ps(f"tp{k}", [P, 4, P]) for k in range(NTP)]
        gram = ps("gram", [P, Q, Q])
        h1_bank = [ps(f"h1_bank{k}", [P, 512]) for k in range(2)]
        h1_ps = [h1_bank[k][:, 0:HM * P].rearrange("p (m b) -> p m b", m=HM) for k in range(2)]
        h2_ps = ps("h2_ps", [P, 512])
        y_ps = ps("y_ps", [P, 512])
        ids_ps_v = [h2_ps, y_ps]
        ids_ps_s = [gram[:, k * HALF:(k + 1) * HALF, :].rearrange("p q c -> p (q c)") for k in range(2)]
        hot_ps = h1_bank

        ids_in = sem("ids_in")
        ident_in_s = sem("ident_in")
        bot_in = sem("bot_in")
        wb_in = sem("wb_in")
        wi_in = sem("wi_in")
        w2_in = sem("w2_in")
        small_in = sem("small_in")
        row_in = [[sem(f"row_in{t}_{g}") for g in range(NG)] for t in range(T)]
        ids_hot_in = sem("ids_hot_in")
        hot_row_in_s = sem("hot_row_in_s")
        mask_in_s = sem("mask_in_s")
        tab_in = [sem(f"tab_in{k}") for k in range(3)]
        ids_cast = sem("ids_cast")
        ids_spread = sem("ids_spread")
        hi_ready = sem("hi_ready")
        lo_ready = sem("lo_ready")
        onehot_v_ready = sem("onehot_v_ready")
        onehot_s_ready = sem("onehot_s_ready")
        distance_ready = sem("distance_ready")
        onehot_used = sem("onehot_used")
        hot_copied = sem("hot_copied")
        turned = sem("turned")
        tp_copied_v = sem("tp_copied_v")
        tp_copied_s = sem("tp_copied_s")
        wbs_ready = sem("wbs_ready")
        z_zeroed = sem("z_zeroed")
        gram_ready = sem("gram_ready")
        far_columns = sem("far_columns")
        packed = sem("packed")
        h1_done = sem("h1_done")
        h1_v_ready = sem("h1_v_ready")
        h1_s_ready = sem("h1_s_ready")
        h2_done = sem("h2_done")
        h2_ready = sem("h2_ready")
        y_done = sem("y_done")
        y_ready = sem("y_ready")
        out_done = sem("out_done")

        def bank(t, g):
            return 1 + t * NG + g

        def copied_by(n):
            return (tp_copied_v, n // 2 + 1) if n % 2 == 0 else (tp_copied_s, (n + 1) // 2)

        def evacuate(copy, eng, n):
            eng.wait_ge(turned, n + 1)
            if n == 0:
                return copy(bot_t[:, :, :], tp[0][:, 0:T, :])
            t, g = (n - 1) // NG, (n - 1) % NG
            fs = GROUPS[g]
            src = tp[n % NTP][:, 0:len(fs), :].rearrange("d f b -> d b f")
            return copy(xt[:, t, :, fs[0]:fs[-1] + 1], src)

        def pack_operands(t, s, g, first):
            n = len(range(g, SLOTS, PACK))
            src = gram[Q * s:Q * s + F, :, first + g:first + g + PACK * (n - 1) + 1:PACK].rearrange("i q c -> i c q")
            return z[Q * g:Q * g + F, t % 2, 0:n, Q * s:Q * s + Q], src, n

        block = ctx.enter_context(nc.Block())

        @block.sync
        def _(sp):
            sp.dma_start(ids_sb[:, :, :], ids.rearrange("(t p) f -> p t f", p=P)).then_inc(ids_in, 16)
            sp.dma_start(ids_i[:, :], ids_hot).then_inc(ids_hot_in, 16)
            sp.dma_start(ident[:, :], ident_in).then_inc(ident_in_s, 16)
            sp.dma_start(hot_row[:, :], hot_row_in).then_inc(hot_row_in_s, 16)

            def load_table(n):
                src = tables[hot[n]].rearrange("(p c) d -> p (c d)", c=chunks[n])
                for p0, p1 in ((0, R // 16 * 16), (R // 16 * 16, R)):
                    sp.dma_start(tab[p0:p1, n % 3, 0:chunks[n] * D], src[p0:p1, :]).then_inc(tab_in[n % 3], 16)

            for n in range(min(3, H)):
                load_table(n)
            sp.dma_start(bot[:, :, :], bottom.rearrange("(t p) d -> p t d", p=P)).then_inc(bot_in, 16)
            sp.dma_start(wb[:, :, :], w_bottom).then_inc(wb_in, 16)
            sp.dma_start(wi[:, :, :], w_inter).then_inc(wi_in, 16)
            sp.dma_start(w2_sb[:, :, :], w2).then_inc(w2_in, 16)
            sp.dma_start(w3_sb[:, :], w3).then_inc(small_in, 16)
            sp.dma_start(b1_sb[:, :], b1).then_inc(small_in, 16)
            sp.dma_start(b2_sb[:, :], b2).then_inc(small_in, 16)
            sp.dma_start(mask[:, :], mask_in).then_inc(mask_in_s, 16)
            for n in range(3, H):
                sp.wait_ge(hi_ready, n - 2)
                sp.wait_ge(lo_ready, n - 2)
                load_table(n)
            sp.wait_ge(y_ready, T)
            sp.dma_start(out.rearrange("b o -> o b"), y_sb[:, :]).then_inc(out_done, 16)
            sp.wait_ge(out_done, 16)

        @block.gpsimd
        def _(pool):
            pool.wait_ge(ids_in, 16)
            for t in range(T):
                for g, fs in enumerate(GROUPS):
                    for k in fs:
                        f = gathered[k]
                        pool.indirect_dma_start(
                            rows[:, t, k, :], None, tables[f],
                            bass.IndirectOffsetOnAxis(ap=ids_sb[:, t, f:f + 1], axis=0),
                        ).then_inc(row_in[t][g], 16)

        @block.tensor
        def _(pe):
            def spread_ids(n):
                if n == 0:
                    pe.wait_ge(ids_cast, 2)
                if n >= 2:
                    pe.wait_ge(onehot_v_ready, made_before(by_vector, n - 1))
                    pe.wait_ge(onehot_s_ready, made_before(by_scalar, n - 1))
                pe.matmul(ids_ps_v[n % 2][0:R, :], spread[:, n, 0:R], ids_r[:, :], start=True, stop=True)
                pe.matmul(ids_ps_s[n % 2][0:R, :], spread[:, n, 0:R], ids_r[:, :],
                          start=True, stop=True).then_inc(ids_spread, 1)

            for n in range(min(2, H)):
                spread_ids(n)
            for n in range(H):
                pe.wait_ge(hi_ready, n + 1)
                pe.wait_ge(lo_ready, n + 1)
                if n >= 2:
                    pe.wait_ge(hot_copied, n - 1)
                for c in range(chunks[n]):
                    if (n, c) in by_vector:
                        j = by_vector.index((n, c))
                        pe.wait_ge(onehot_v_ready, j + 1)
                        onehot = onehot_v[:, j % NOV, :]
                    else:
                        j = by_scalar.index((n, c))
                        pe.wait_ge(onehot_s_ready, j + 1)
                        onehot = onehot_s[:, j % NOS, :]
                    cols = slice(c * D, (c + 1) * D)
                    pe.matmul(hot_ps[n % 2][:, :], tab_hi[:, n % 3, cols], onehot, start=(c == 0), stop=False)
                    pe.matmul(hot_ps[n % 2][:, :], tab_lo[:, n % 3, cols], onehot,
                              start=False, stop=(c == chunks[n] - 1)).then_inc(onehot_used, 1)
                if n + 2 < H:
                    spread_ids(n + 2)

            pe.wait_ge(ident_in_s, 16)
            pe.wait_ge(bot_in, 16)
            for t in range(T):
                last = pe.transpose(tp[0][:, t, :], bot[:, t, :], ident[:, :])
            last.then_inc(turned, 1)

            def turn(t, groups):
                for g in groups:
                    n = bank(t, g)
                    if n >= NTP:
                        pe.wait_ge(*copied_by(n - NTP))
                    pe.wait_ge(row_in[t][g], 16 * len(GROUPS[g]))
                    for k, f in enumerate(GROUPS[g]):
                        last = pe.transpose(tp[n % NTP][:, k, :], rows[:, t, f, :], ident[:, :])
                    last.then_inc(turned, 1)

            def grams(t):
                pe.wait_ge(*copied_by(bank(t, NG - 1)))
                pe.wait_ge(*copied_by(bank(t, NG - 2)))
                if t == 0:
                    pe.wait_ge(hot_copied, H)
                    pe.wait_ge(onehot_s_ready, len(by_scalar))
                if t >= 1:
                    pe.wait_ge(packed, PACK * t)
                for pair in (range(0, PACK // 2), range(PACK // 2, PACK)):
                    for q in range(Q):
                        for s in pair:
                            x = xt[:, t, Q * s + q, :]
                            last = pe.matmul(gram[Q * s:Q * s + F, q, 0:F], x, x, start=True, stop=True)
                    last.then_inc(gram_ready, 1)

            def layer1(t):
                if t == 0:
                    pe.wait_ge(wbs_ready, 1)
                    pe.wait_ge(wi_in, 16)
                    pe.wait_ge(*copied_by(0))
                pe.wait_ge(packed, PACK * (t + 1))
                for half in range(2):
                    if t >= 1:
                        pe.wait_ge(h1_s_ready if half == 0 else h1_v_ready, t)
                    for k in range(HM):
                        cols = slice((half * HM + k) * P, (half * HM + k + 1) * P)
                        pe.matmul(h1_ps[half][:, k, :], wbs[:, cols], bot_t[:, t, :], start=True, stop=False)
                        for c in range(NC):
                            r = Q * len(range(PACK * c, min(PACK * c + PACK, SLOTS)))
                            last = pe.matmul(h1_ps[half][:, k, :], wi[0:r, c, cols], z[0:r, t % 2, c, :],
                                             start=False, stop=(c == NC - 1))
                    last.then_inc(h1_done, 1)

            def layer2(t):
                if t == 0:
                    pe.wait_ge(w2_in, 16)
                pe.wait_ge(h1_s_ready, t + 1)
                pe.wait_ge(h1_v_ready, t + 1)
                if t == 0:
                    pe.wait_ge(onehot_v_ready, len(by_vector))
                if t >= 1:
                    pe.wait_ge(h2_ready, t)
                for m in range(M2):
                    for c in range(M1):
                        last = pe.matmul(h2_ps[:, m * P:(m + 1) * P], w2_sb[:, c, m * P:(m + 1) * P],
                                         h1[:, t % 2, c, :], start=(c == 0), stop=(c == M1 - 1))
                last.then_inc(h2_done, 1)

            def layer3(t):
                if t == 0:
                    pe.wait_ge(small_in, 48)
                pe.wait_ge(h2_ready, t + 1)
                if t >= 1:
                    pe.wait_ge(y_ready, t)
                for m in range(M2):
                    last = pe.matmul(y_ps[0:1, 0:P], w3_sb[:, m:m + 1], h2[:, t % 2, m, :],
                                     start=(m == 0), stop=(m == M2 - 1))
                last.then_inc(y_done, 1)

            for t in range(T + 2):
                if t < T:
                    turn(t, EARLY)
                if 1 <= t <= T:
                    layer1(t - 1)
                if t >= 2:
                    layer3(t - 2)
                if t < T:
                    turn(t, LATE)
                    grams(t)
                if 1 <= t <= T:
                    layer2(t - 1)

        @block.vector
        def _(dve):
            dve.wait_ge(ids_hot_in, 16)
            dve.tensor_copy(ids_r[:, :], ids_i[:, :]).then_inc(ids_cast, 1)
            dve.memset(z[:, :, :, :], 0.0).then_inc(z_zeroed, 1)

            def split_low(n):
                dve.wait_ge(hi_ready, n + 1)
                if n >= 3:
                    dve.wait_ge(onehot_used, before[n - 2])
                w = chunks[n] * D
                dve.tensor_tensor(tab_lo[:, n % 3, 0:w], tab[:, n % 3, 0:w], tab_hi[:, n % 3, 0:w].bitcast(F32),
                                  ALU.subtract).then_inc(lo_ready, 1)

            dve.wait_ge(hot_row_in_s, 16)
            for n in range(H):
                dve.wait_ge(ids_spread, n + 1)
                for c in range(chunks[n]):
                    if n == 0 and c == 0:
                        split_low(0)
                    if n + 1 < H and c == chunks[n] // 2:
                        split_low(n + 1)
                    if (n, c) not in by_vector:
                        continue
                    j = by_vector.index((n, c))
                    if j >= NOV:
                        dve.wait_ge(onehot_used, chunk_number(by_vector, j - NOV) + 1)
                    dve.tensor_scalar(onehot_v[:, j % NOV, :], ids_ps_v[n % 2][0:R, :],
                                      hot_row[0:R, 0, chunks[n] != MAXC, c:c + 1], None,
                                      ALU.is_equal).then_inc(onehot_v_ready, 1)
            evacuate(dve.tensor_copy, dve, 0).then_inc(tp_copied_v, 1)
            dve.wait_ge(wb_in, 16)
            dve.tensor_tensor(wbs[:, :], wb[:, 0, :], wb[:, 1, :], ALU.add).then_inc(wbs_ready, 1)

            def move(t, groups):
                for g in groups:
                    if bank(t, g) % 2 == 0:
                        evacuate(dve.tensor_copy, dve, bank(t, g)).then_inc(tp_copied_v, 1)

            def near_columns(t):
                if t == 0:
                    dve.wait_ge(mask_in_s, 16)
                for s in range(PACK):
                    dve.wait_ge(far_columns, PACK * t + s + 1)
                    for g in range(PACK):
                        cells, columns, n = pack_operands(t, s, g, 0)
                        where = mask[Q * g:Q * g + F, 0:n].unsqueeze(2).broadcast_to([F, n, Q])
                        last = dve.copy_predicated(cells, where, columns)
                    last.then_inc(packed, 1)

            def hidden1(t):
                if t == 0:
                    dve.wait_ge(small_in, 48)
                dve.wait_ge(h1_done, 2 * t + 2)
                if t >= 2:
                    dve.wait_ge(h2_done, t - 1)
                for k in range(HM):
                    last = dve.tensor_scalar(h1[:, t % 2, HM + k, :], h1_ps[1][:, k, :], b1_sb[:, HM + k:HM + k + 1],
                                             0.0, ALU.add, ALU.max)
                last.then_inc(h1_v_ready, 1)

            def hidden2(t):
                dve.wait_ge(h2_done, t + 1)
                if t >= 2:
                    dve.wait_ge(y_done, t - 1)
                for m in range(M2):
                    last = dve.tensor_scalar(h2[:, t % 2, m, :], h2_ps[:, m * P:(m + 1) * P],
                                             b2_sb[:, m:m + 1], 0.0, ALU.add, ALU.max)
                last.then_inc(h2_ready, 1)

            def output(t):
                dve.wait_ge(y_done, t + 1)
                dve.tensor_copy(y_sb[0:1, t * P:(t + 1) * P], y_ps[0:1, 0:P]).then_inc(y_ready, 1)

            for t in range(T + 2):
                if t < T:
                    move(t, EARLY)
                if 1 <= t <= T:
                    hidden1(t - 1)
                if t >= 2:
                    output(t - 2)
                if t < T:
                    move(t, LATE)
                    near_columns(t)
                if 1 <= t <= T:
                    hidden2(t - 1)

        @block.scalar
        def _(act):
            def split_high(n):
                act.wait_ge(tab_in[n % 3], 32 * (n // 3 + 1))
                if n >= 3:
                    act.wait_ge(onehot_used, before[n - 2])
                w = chunks[n] * D
                act.copy(tab_hi[:, n % 3, 0:w], tab[:, n % 3, 0:w]).then_inc(hi_ready, 1)

            act.wait_ge(ident_in_s, 16)
            act.copy(spread[:, :, :], ident[0:H, 0:H].unsqueeze(2).broadcast_to([H, H, P])).then_inc(ids_cast, 1)
            for n in range(H):
                if n == 0:
                    split_high(0)
                    split_high(1)
                if n + 2 < H:
                    split_high(n + 2)
                for j in range(made_before(by_scalar, n), made_before(by_scalar, n + 1)):
                    c = by_scalar[j][1]
                    if n == 0 and j == 0:
                        act.wait_ge(hot_row_in_s, 16)
                    act.wait_ge(ids_spread, n + 1)
                    act.activation(distance[:, j % NOS, :], ids_ps_s[n % 2][0:R, :], ACT.Abs,
                                   bias=hot_row[0:R, 1, chunks[n] != MAXC, c:c + 1]).then_inc(distance_ready, 1)
                    act.wait_ge(distance_ready, j + 1)
                    if j >= NOS:
                        act.wait_ge(onehot_used, chunk_number(by_scalar, j - NOS) + 1)
                    act.activation(onehot_s[:, j % NOS, :], distance[:, j % NOS, :], ACT.Relu,
                                   bias=1.0, scale=-1.0).then_inc(onehot_s_ready, 1)
                act.wait_ge(onehot_used, before[n + 1])
                act.copy(xt[:, :, :, G + n], hot_ps[n % 2][:, :].rearrange("d (t b) -> d t b", t=T)).then_inc(hot_copied, 1)

            def move(t, groups):
                for g in groups:
                    if bank(t, g) % 2 == 1:
                        evacuate(act.copy, act, bank(t, g)).then_inc(tp_copied_s, 1)

            def all_far_columns(t):
                if t == 0:
                    act.wait_ge(z_zeroed, 1)
                if t >= 2:
                    act.wait_ge(h1_done, 2 * (t - 1))
                for s in range(PACK):
                    act.wait_ge(gram_ready, 2 * t + s // (PACK // 2) + 1)
                    for g in range(PACK):
                        cells, columns, _ = pack_operands(t, s, g, HF)
                        last = act.copy(cells, columns)
                    last.then_inc(far_columns, 1)

            def hidden1(t):
                if t == 0:
                    act.wait_ge(small_in, 48)
                act.wait_ge(h1_done, 2 * t + 1)
                if t >= 2:
                    act.wait_ge(h2_done, t - 1)
                for k in range(HM):
                    last = act.activation(h1[:, t % 2, k, :], h1_ps[0][:, k, :], ACT.Relu, bias=b1_sb[:, k:k + 1])
                last.then_inc(h1_s_ready, 1)

            for t in range(T + 1):
                if t < T:
                    move(t, EARLY)
                if t >= 1:
                    hidden1(t - 1)
                if t < T:
                    move(t, LATE)
                    all_far_columns(t)


def kernel(**inputs):
    import numpy as np
    import concourse.bacc as bacc
    from concourse.bass_utils import run_bass_kernel_spmd

    nc = bacc.Bacc("TRN2", target_bir_lowering=False, num_devices=1)
    w1 = np.asarray(inputs["W_top1"])
    n1 = w1.shape[1]
    tables = [np.asarray(inputs[f"tbl_{f}"]) for f in range(F)]
    hot = sorted(sorted(range(F), key=lambda f: (tables[f].shape[0], f))[:HOT])
    gathered = [f for f in range(F) if f not in hot]
    order = gathered + hot
    w_inter = np.zeros((P, NC, n1), w1.dtype)
    mask = np.zeros((P, NC), np.int32)
    for k in range(SLOTS):
        for r in range(F):
            far = k <= r < k + HF
            mask[Q * (k % PACK) + r, k // PACK] = not far
            if far or (k < SLOTS - 1 and r != k + HF):
                i, j = order[r], order[k + HF if far else k]
                i, j = max(i, j), min(i, j)
                w_inter[Q * (k % PACK) + r, k // PACK] = w1[D + i * (i - 1) // 2 + j]
    c, p = np.arange(MAXC), np.arange(P)[:, None]
    hot_row = np.stack([p * MAXC + c, p * 8 + c], axis=1)
    hot_row = np.stack([hot_row, -hot_row], axis=1).astype(np.float32)
    w_bottom = np.ascontiguousarray(np.stack([w1[:D], w1[-D:]], axis=1))

    def columns(a):
        a = np.asarray(a)
        return np.ascontiguousarray(a.reshape((a.shape[0] // P, P) + a.shape[1:]).swapaxes(0, 1))

    arrays = {
        "bottom": np.asarray(inputs["r_bottom_mlp_out"]), "ids": np.asarray(inputs["ids"]),
        "w_bottom": w_bottom, "w_inter": w_inter, "b1": columns(inputs["b_top1"]),
        "w2": columns(inputs["W_top2"]), "b2": columns(inputs["b_top2"]),
        "w3": columns(np.asarray(inputs["W_top3"])[:, 0]), "ident": np.eye(P, dtype=np.float32),
    }
    arrays["ids_hot"] = np.ascontiguousarray(arrays["ids"].T[hot])
    arrays["hot_row"] = hot_row
    arrays["mask"] = mask
    for f in range(F):
        arrays[f"tbl_{f}"] = tables[f]
    ap = {k: nc.dram_tensor(k + "_dram", a.shape, mybir.dt.from_np(a.dtype), kind="ExternalInput").ap() for k, a in arrays.items()}
    out = nc.dram_tensor("y_dram", (arrays["bottom"].shape[0], 1), F32, kind="ExternalOutput").ap()
    build_tower(nc, ap["bottom"], ap["ids"], ap["ids_hot"], [ap[f"tbl_{f}"] for f in range(F)], gathered, hot,
                ap["w_bottom"], ap["w_inter"],
                ap["b1"], ap["w2"], ap["b2"], ap["w3"], ap["ident"], ap["hot_row"], ap["mask"], out)
    r = run_bass_kernel_spmd(nc, [{k + "_dram": a for k, a in arrays.items()}], core_ids=[0])
    return r.results[0]["y_dram"]
```

```python
from contextlib import ExitStack

import concourse.bass as bass
from concourse import mybir

F32 = mybir.dt.float32
I32 = mybir.dt.int32
ALU = mybir.AluOpType
ACT = mybir.ActivationFunctionType
F32R = mybir.dt.float32r

P = 128
Q = 32
F = 27
D = 128
PACK = P // Q
HF = (F - 1) // 2
SLOTS = HF + 1
NC = (SLOTS + PACK - 1) // PACK
SPARE = Q - F
R = 125
MAXC = 10
GROUP = 3
HOT = 8
EARLY = (0, 0, 2, 2, 2, 1, 1, 2)
AHEAD = ((0, 1, 2, 0, 0), (0, 0, 1, 0, 0), (2, 0, 1, 0, 0), (2, 0, 1, 1, 1))


def bottom_places():
    places, first = [], 0
    used = SLOTS % PACK
    if used:
        places.append((0, Q * (PACK - used), Q * used, NC - 1))
        first = Q * (PACK - used)
    for k in range(SLOTS):
        count = min(SPARE, D - first)
        if count > 0:
            places.append((first, count, Q * (k % PACK) + F, k // PACK))
            first += count
    assert first == D
    return places


def build_tower(nc, bottom, ids, ids_hot, tables, gathered, hot, w_bottom, w_inter, b1, w2, b2, w3,
                ident_in, hot_row_in, mask_in, out):
    B = bottom.shape[0]
    T = B // P
    N1 = w_inter.shape[2]
    M1 = N1 // P
    N2 = w2.shape[2]
    M2 = N2 // P
    G = len(gathered)
    H = len(hot)
    GROUPS = [[list(range(f, min(f + 4, G))) for f in range(0, G, 4)] for t in range(T)]
    if len(GROUPS[T - 1][-1]) > 1:
        GROUPS[T - 1].append([GROUPS[T - 1][-1].pop()])
    NG = len(GROUPS[0])
    NROWS = 3
    NTAB = 3
    chunks = [tables[f].shape[0] // R for f in hot]
    WT = max(chunks) * D
    before = [sum(chunks[:n]) for n in range(H + 1)]
    NGROUP = 2
    by_vector, by_scalar = [], []
    for n in range(H):
        by_vector += [(n, range(0, GROUP)), (n, range(2 * GROUP, 8))]
        if chunks[n] > 8:
            by_vector += [(n, range(8, chunks[n]))]
        by_scalar += [(n, range(GROUP, 2 * GROUP))]

    def group_of(made, n, c):
        return next(((j, c - some[0]) for j, (m, some) in enumerate(made) if m == n and c in some), None)

    def used_up(made, j):
        n, some = made[j]
        return before[n] + some[-1] + 1

    def made_before(made, n):
        return sum(m < n for m, _ in made)

    with ExitStack() as ctx:
        def sb(name, shape, dt=F32):
            return ctx.enter_context(nc.sbuf_tensor(name, shape, dt))

        def ps(name, shape):
            return ctx.enter_context(nc.psum_tensor(name, shape, F32))

        def sem(name):
            return ctx.enter_context(nc.semaphore(name))

        ids_sb = sb("ids_sb", [P, T, F], I32)
        rows = sb("rows", [P, NROWS, G, D])
        xt = sb("xt", [D, T, P, F])
        bot = sb("bot", [P, T, D])
        bot_t = sb("bot_t", [D, T, P])
        ident = sb("ident", [P, P])
        wb = sb("wb", [P, 2, N1])
        wbs = sb("wbs", [P, N1])
        wi = sb("wi", [P, NC, N1])
        w2_sb = sb("w2_sb", [P, M1, N2])
        w3_sb = sb("w3_sb", [P, M2])
        b1_sb = sb("b1_sb", [P, M1])
        b2_sb = sb("b2_sb", [P, M2])
        z = sb("z", [P, NC, T, P])
        h1 = sb("h1", [P, 2, M1, P])
        h2 = sb("h2", [P, 2, M2, P])
        y_sb = sb("y_sb", [1, B])
        mask = sb("mask", [P, NC], I32)
        hot_row = sb("hot_row", [P, 2, 2, MAXC])
        ids_i = sb("ids_i", [H, B], I32)
        ids_r = sb("ids_r", [H, B], F32R)
        spread = sb("spread", [H, H], F32R)
        tab = sb("tab", [R, NTAB, WT])
        tab_hi = sb("tab_hi", [R, 3, WT], F32R)
        tab_lo = sb("tab_lo", [R, 3, WT], F32R)
        onehot_v = sb("onehot_v", [R, NGROUP, GROUP, B], F32R)
        onehot_s = sb("onehot_s", [R, NGROUP, GROUP, B], F32R)
        ids_all = sb("ids_all", [R, NTAB, B], I32)
        distance = sb("distance", [R, GROUP, B])

        NTP = 2
        HM = M1 // 2
        tp = [ps(f"tp{k}", [P, 4, P]) for k in range(NTP)]
        gram = ps("gram", [P, Q, Q])
        h1_bank = [ps(f"h1_bank{k}", [P, 512]) for k in range(2)]
        h1_ps = [h1_bank[k][:, 0:HM * P].rearrange("p (m b) -> p m b", m=HM) for k in range(2)]
        h2_ps = ps("h2_ps", [P, 512])
        y_ps = ps("y_ps", [P, 512])
        ids_ps = [h2_ps, y_ps]
        hot_ps = h1_bank
        last_h2_ps = [h2_ps[:, 0:P], tp[0][:, 0, :]]
        last_y_ps = tp[1][0:1, 0, :]

        first_ids_in = sem("first_ids_in")
        ids_in = sem("ids_in")
        ident_in_s = sem("ident_in")
        bot_in = sem("bot_in")
        wb_in = sem("wb_in")
        wi_in = sem("wi_in")
        w2_in = sem("w2_in")
        small_in = sem("small_in")
        row_in = [[sem(f"row_in{t}_{g}") for g in range(len(GROUPS[t]))] for t in range(T)]
        ids_hot_in = sem("ids_hot_in")
        hot_row_in_s = sem("hot_row_in_s")
        mask_in_s = sem("mask_in_s")
        tab_in = [sem(f"tab_in{k}") for k in range(NTAB)]
        ids_cast = sem("ids_cast")
        ids_spread = sem("ids_spread")
        ids_all_in = [sem(f"ids_all_in{k}") for k in range(NTAB)]
        hi_ready = sem("hi_ready")
        lo_ready = sem("lo_ready")
        onehot_v_ready = sem("onehot_v_ready")
        onehot_s_ready = sem("onehot_s_ready")
        distance_ready = sem("distance_ready")
        onehot_used = sem("onehot_used")
        hot_copied = sem("hot_copied")
        turned = sem("turned")
        tp_copied_v = sem("tp_copied_v")
        tp_copied_s = sem("tp_copied_s")
        wbs_ready = sem("wbs_ready")
        wbs_placed = sem("wbs_placed")
        bottom_placed = sem("bottom_placed")
        z_zeroed = sem("z_zeroed")
        gram_ready = sem("gram_ready")
        far_columns = sem("far_columns")
        packed = sem("packed")
        h1_done = sem("h1_done")
        h1_s_ready = sem("h1_s_ready")
        h1_v_ready = sem("h1_v_ready")
        h2_done = sem("h2_done")
        h2_ready = sem("h2_ready")
        y_done = sem("y_done")
        y_ready = sem("y_ready")
        last_h2_done = sem("last_h2_done")
        last_h2_ready = [sem(f"last_h2_ready{m}") for m in range(M2)]
        out_done = sem("out_done")

        def bank(t, g):
            return 1 + t * NG + g

        early_before = [sum(EARLY[:n]) for n in range(H + 1)]
        assert early_before[H] + sum(map(sum, AHEAD)) == bank(T - 1, len(GROUPS[T - 1]))

        def early(n):
            return range(early_before[n], early_before[n + 1])

        def ahead(t, parts):
            first = early_before[H] + sum(map(sum, AHEAD[:t]))
            return range(first + sum(AHEAD[t][:parts[0]]), first + sum(AHEAD[t][:parts[-1] + 1]))

        def copied_by(n):
            return (tp_copied_v, n // 2 + 1) if n % 2 == 0 else (tp_copied_s, (n + 1) // 2)

        def evacuate(copy, eng, n):
            eng.wait_ge(turned, n + 1)
            if n == 0:
                return copy(bot_t[:, :, :], tp[0][:, 0:T, :])
            t = min((n - 1) // NG, T - 1)
            g = n - bank(t, 0)
            fs = GROUPS[t][g]
            src = tp[n % NTP][:, 0:len(fs), :].rearrange("d f b -> d b f")
            return copy(xt[:, t, :, fs[0]:fs[-1] + 1], src)

        def pack_operands(t, s, g, first, slots):
            n = len(range(g, slots, PACK))
            src = gram[Q * s:Q * s + F, :, first + g:first + g + PACK * (n - 1) + 1:PACK].rearrange("i q c -> i c q")
            return z[Q * g:Q * g + F, 0:n, t, Q * s:Q * s + Q], src, n

        block = ctx.enter_context(nc.Block())

        @block.sync
        def _(sp):
            sp.dma_start(ids_sb[:, 0, :], ids[0:P, :]).then_inc(first_ids_in, 16)

            def load_table(n):
                src = tables[hot[n]].rearrange("(p c) d -> p (c d)", c=chunks[n])
                for p0, p1 in ((0, R // 16 * 16), (R // 16 * 16, R)):
                    sp.dma_start(tab[p0:p1, n % NTAB, 0:chunks[n] * D], src[p0:p1, :]).then_inc(tab_in[n % NTAB], 16)

            def load_ids(n):
                sp.dma_start(ids_all[:, n % NTAB, :],
                             ids_hot[n:n + 1, :].broadcast_to([R, B])).then_inc(ids_all_in[n % NTAB], 16)

            sp.dma_start(ids_i[:, :], ids_hot).then_inc(ids_hot_in, 16)
            sp.dma_start(ident[:, :], ident_in).then_inc(ident_in_s, 16)
            load_table(0)
            sp.dma_start(hot_row[:, :, :, :], hot_row_in).then_inc(hot_row_in_s, 16)
            sp.dma_start(ids_sb[:, 1:T, :], ids[P:B, :].rearrange("(t p) f -> p t f", p=P)).then_inc(ids_in, 16)
            load_ids(0)
            for n in range(1, min(NTAB, H)):
                load_table(n)
                load_ids(n)
            sp.dma_start(bot[:, :, :], bottom.rearrange("(t p) d -> p t d", p=P)).then_inc(bot_in, 16)
            sp.dma_start(wb[:, :, :], w_bottom).then_inc(wb_in, 16)
            for n in range(NTAB, H):
                sp.wait_ge(hi_ready, n - NTAB + 1)
                sp.wait_ge(lo_ready, n - NTAB + 1)
                load_table(n)
                sp.wait_ge(onehot_s_ready, n - NTAB + 1)
                load_ids(n)
            sp.dma_start(wi[:, :, :], w_inter).then_inc(wi_in, 16)
            sp.dma_start(mask[:, :], mask_in).then_inc(mask_in_s, 16)
            sp.wait_ge(z_zeroed, 1)
            sp.wait_ge(*copied_by(0))
            for row, count, p, c in bottom_places():
                sp.dma_start(z[p:p + count, c, :, :], bot_t[row:row + count, :, :]).then_inc(bottom_placed, 16)
            sp.wait_ge(wi_in, 16)
            sp.wait_ge(wbs_ready, 1)
            for row, count, p, c in bottom_places():
                sp.dma_start(wi[p:p + count, c, :], wbs[row:row + count, :]).then_inc(wbs_placed, 16)
            sp.dma_start(b1_sb[:, :], b1).then_inc(small_in, 16)
            sp.dma_start(b2_sb[:, :], b2).then_inc(small_in, 16)
            sp.dma_start(w3_sb[:, :], w3).then_inc(small_in, 16)
            sp.dma_start(w2_sb[:, :, :], w2).then_inc(w2_in, 16)
            sp.wait_ge(y_ready, T)
            sp.dma_start(out.rearrange("b o -> o b"), y_sb[:, :]).then_inc(out_done, 16)
            sp.wait_ge(out_done, 16)

        @block.gpsimd
        def _(pool):
            pool.wait_ge(first_ids_in, 16)
            for t in range(T):
                if t == 1:
                    pool.wait_ge(ids_in, 16)
                for g, fs in enumerate(GROUPS[t]):
                    if t >= NROWS:
                        pool.wait_ge(turned, bank(t - NROWS, min(g, NG - 1)) + 1)
                    for k in fs:
                        f = gathered[k]
                        pool.indirect_dma_start(
                            rows[:, t % NROWS, k, :], None, tables[f],
                            bass.IndirectOffsetOnAxis(ap=ids_sb[:, t, f:f + 1], axis=0),
                        ).then_inc(row_in[t][g], 16)

        @block.tensor
        def _(pe):
            def spread_ids(n):
                if n == 0:
                    pe.wait_ge(ids_cast, 2)
                if n >= 2:
                    pe.wait_ge(onehot_v_ready, made_before(by_vector, n - 1))
                pe.matmul(ids_ps[n % 2][0:R, :], spread[:, n:n + 1].broadcast_to([H, R]), ids_r[:, :], start=True,
                          stop=True).then_inc(ids_spread, 1)

            def turn_bank(n):
                if n >= NTP:
                    pe.wait_ge(*copied_by(n - NTP))
                if n == 0:
                    pe.wait_ge(ident_in_s, 16)
                    pe.wait_ge(bot_in, 16)
                    sources = [bot[:, t, :] for t in range(T)]
                else:
                    t = min((n - 1) // NG, T - 1)
                    g = n - bank(t, 0)
                    pe.wait_ge(row_in[t][g], 16 * len(GROUPS[t][g]))
                    sources = [rows[:, t % NROWS, f, :] for f in GROUPS[t][g]]
                for k, source in enumerate(sources):
                    last = pe.transpose(tp[n % NTP][:, k, :], source, ident[:, :])
                last.then_inc(turned, 1)

            def contract(n, some, part):
                for c in some:
                    if group_of(by_vector, n, c):
                        j, k = group_of(by_vector, n, c)
                        pe.wait_ge(onehot_v_ready, j + 1)
                        onehot = onehot_v[:, j % NGROUP, k, :]
                    else:
                        j, k = group_of(by_scalar, n, c)
                        pe.wait_ge(onehot_s_ready, j + 1)
                        onehot = onehot_s[:, j % NGROUP, k, :]
                    cols = slice(c * D, (c + 1) * D)
                    if part == "hi":
                        pe.matmul(hot_ps[n % 2][:, :], tab_hi[:, n % 3, cols], onehot, start=(c == 0), stop=False)
                    else:
                        pe.wait_ge(lo_ready, n + 1)
                        pe.matmul(hot_ps[n % 2][:, :], tab_lo[:, n % 3, cols], onehot,
                                  start=False, stop=(c == chunks[n] - 1)).then_inc(onehot_used, 1)

            for n in range(min(2, H)):
                spread_ids(n)
            for n in range(H):
                pe.wait_ge(hi_ready, n + 1)
                if n >= 2:
                    pe.wait_ge(hot_copied, n - 1)
                for c in range(chunks[n]):
                    if n > 0 or c >= GROUP:
                        contract(n, [c], "hi")
                        contract(n, [c], "lo")
                    elif c == 0:
                        contract(n, range(GROUP), "hi")
                        contract(n, range(GROUP), "lo")
                    for k, b in enumerate(early(n)):
                        if c == 2 + 3 * k:
                            turn_bank(b)
                if n + 2 < H:
                    spread_ids(n + 2)

            def grams(t, half):
                if half == 0:
                    pe.wait_ge(*copied_by(bank(t, len(GROUPS[t]) - 1)))
                    pe.wait_ge(*copied_by(bank(t, len(GROUPS[t]) - 2)))
                    if t == 0:
                        pe.wait_ge(hot_copied, H)
                pair = range(PACK // 2 * half, PACK // 2 * (half + 1))
                if t >= 1:
                    pe.wait_ge(packed, PACK * (t - 1) + pair[-1] + 1)
                for q in range(Q):
                    for s in pair:
                        x = xt[:, t, Q * s + q, :]
                        last = pe.matmul(gram[Q * s:Q * s + F, q, 0:F], x, x, start=True, stop=True)
                last.then_inc(gram_ready, 1)

            def layer1(t, m):
                if m == 0:
                    if t == 0:
                        pe.wait_ge(wbs_placed, 16 * len(bottom_places()))
                        pe.wait_ge(bottom_placed, 16 * len(bottom_places()))
                    pe.wait_ge(packed, PACK * (t + 1))
                if t >= 1 and m % HM == 0:
                    pe.wait_ge(h1_s_ready if m == 0 else h1_v_ready, t)
                psum, cols = h1_ps[m // HM][:, m % HM, :], slice(m * P, (m + 1) * P)
                for c in range(NC):
                    last = pe.matmul(psum, wi[:, c, cols], z[:, c, t, :], start=(c == 0), stop=(c == NC - 1))
                if m % HM == HM - 1:
                    last.then_inc(h1_done, 1)

            def layer2(t):
                if t == 0:
                    pe.wait_ge(w2_in, 16)
                pe.wait_ge(h1_s_ready, t + 1)
                pe.wait_ge(h1_v_ready, t + 1)
                if t == 0:
                    pe.wait_ge(onehot_v_ready, len(by_vector))
                if t >= 1:
                    pe.wait_ge(h2_ready, t)
                for m in range(M2):
                    for c in range(M1):
                        last = pe.matmul(h2_ps[:, m * P:(m + 1) * P], w2_sb[:, c, m * P:(m + 1) * P],
                                         h1[:, t % 2, c, :], start=(c == 0), stop=(c == M1 - 1))
                last.then_inc(h2_done, 1)

            def layer3(t):
                if t == 0:
                    pe.wait_ge(small_in, 48)
                pe.wait_ge(h2_ready, t + 1)
                if t >= 1:
                    pe.wait_ge(y_ready, t)
                for m in range(M2):
                    last = pe.matmul(y_ps[0:1, 0:P], w3_sb[:, m:m + 1], h2[:, t % 2, m, :],
                                     start=(m == 0), stop=(m == M2 - 1))
                last.then_inc(y_done, 1)

            for t in range(T):
                for n in ahead(t, [0]):
                    turn_bank(n)
                if t >= 1:
                    for m in range(M1):
                        layer1(t - 1, m)
                        for n in ahead(t, [m + 1]):
                            turn_bank(n)
                if t >= 2:
                    layer3(t - 2)
                for half in range(2):
                    grams(t, half)
                    if t == 0:
                        for n in ahead(t, [1 + half]):
                            turn_bank(n)
                if t >= 1:
                    layer2(t - 1)

            t = T - 1
            for m in range(M1):
                layer1(t, m)
            pe.wait_ge(h2_ready, t)
            for c in range(M1):
                if c % HM == 0:
                    pe.wait_ge(h1_s_ready if c == 0 else h1_v_ready, T)
                for m in range(M2):
                    last = pe.matmul(last_h2_ps[m], w2_sb[:, c, m * P:(m + 1) * P], h1[:, t % 2, c, :],
                                     start=(c == 0), stop=(c == M1 - 1))
                    if c == M1 - 1:
                        last.then_inc(last_h2_done, 1)
            layer3(t - 1)
            for m in range(M2):
                pe.wait_ge(last_h2_ready[m], 1)
                last = pe.matmul(last_y_ps, w3_sb[:, m:m + 1], h2[:, t % 2, m, :],
                                 start=(m == 0), stop=(m == M2 - 1))
            last.then_inc(y_done, 1)

        @block.vector
        def _(dve):
            dve.wait_ge(ids_hot_in, 16)
            dve.tensor_copy(ids_r[:, :], ids_i[:, :]).then_inc(ids_cast, 1)
            dve.memset(z[0:Q * (SLOTS % PACK), NC - 1, :, :], 0.0).then_inc(z_zeroed, 1)

            def split_low(n):
                dve.wait_ge(hi_ready, n + 1)
                if n >= 3:
                    dve.wait_ge(onehot_used, before[n - 2])
                w = chunks[n] * D
                dve.tensor_tensor(tab_lo[:, n % 3, 0:w], tab[:, n % NTAB, 0:w], tab_hi[:, n % 3, 0:w].bitcast(F32),
                                  ALU.subtract).then_inc(lo_ready, 1)

            def move_banks(banks):
                for n in banks:
                    if n % 2 == 0:
                        evacuate(dve.tensor_copy, dve, n).then_inc(tp_copied_v, 1)

            dve.wait_ge(hot_row_in_s, 16)
            for n in range(H):
                dve.wait_ge(ids_spread, n + 1)
                for j in range(made_before(by_vector, n), made_before(by_vector, n + 1)):
                    some = by_vector[j][1]
                    if some[0] == 2 * GROUP and 0 < n < H - 1:
                        split_low(n + 1)
                    if j >= NGROUP:
                        dve.wait_ge(onehot_used, used_up(by_vector, j - NGROUP))
                    table_rows = hot_row[0:R, 0, int(chunks[n] != MAXC), some[0]:some[-1] + 1]
                    dve.tensor_tensor(onehot_v[:, j % NGROUP, 0:len(some), :],
                                      ids_ps[n % 2][0:R, :].unsqueeze(1).broadcast_to([R, len(some), B]),
                                      table_rows.unsqueeze(2).broadcast_to([R, len(some), B]),
                                      ALU.is_equal).then_inc(onehot_v_ready, 1)
                    if n == 0 and j < 2:
                        split_low(j)
                move_banks(early(n))
                if n == 2:
                    dve.wait_ge(wb_in, 16)
                    dve.tensor_tensor(wbs[:, :], wb[:, 0, :], wb[:, 1, :], ALU.add).then_inc(wbs_ready, 1)

            def near_columns(t):
                if t == 0:
                    dve.wait_ge(mask_in_s, 16)
                for s in range(PACK):
                    dve.wait_ge(far_columns, PACK * t + s + 1)
                    for g in range(PACK):
                        cells, columns, n = pack_operands(t, s, g, 0, SLOTS - 1)
                        where = mask[Q * g:Q * g + F, 0:n].unsqueeze(2).broadcast_to([F, n, Q])
                        last = dve.copy_predicated(cells, where, columns)
                    last.then_inc(packed, 1)

            def hidden1(t):
                if t == 0:
                    dve.wait_ge(small_in, 48)
                dve.wait_ge(h1_done, 2 * t + 2)
                if t >= 2:
                    dve.wait_ge(h2_done, t - 1)
                for k in range(HM):
                    last = dve.tensor_scalar(h1[:, t % 2, HM + k, :], h1_ps[1][:, k, :], b1_sb[:, HM + k:HM + k + 1],
                                             0.0, ALU.add, ALU.max)
                last.then_inc(h1_v_ready, 1)

            def hidden2(t):
                dve.wait_ge(h2_done, t + 1)
                if t >= 2:
                    dve.wait_ge(y_done, t - 1)
                for m in range(M2):
                    last = dve.tensor_scalar(h2[:, t % 2, m, :], h2_ps[:, m * P:(m + 1) * P],
                                             b2_sb[:, m:m + 1], 0.0, ALU.add, ALU.max)
                last.then_inc(h2_ready, 1)

            def output(t):
                dve.wait_ge(y_done, t + 1)
                source = y_ps[0:1, 0:P] if t < T - 1 else last_y_ps
                dve.tensor_copy(y_sb[0:1, t * P:(t + 1) * P], source).then_inc(y_ready, 1)

            for t in range(T):
                if t == 0:
                    move_banks(ahead(t, range(2)))
                    near_columns(t)
                    move_banks(ahead(t, [2]))
                    continue
                move_banks(ahead(t, range(M1)))
                hidden1(t - 1)
                if t >= 2:
                    output(t - 2)
                move_banks(ahead(t, [M1]))
                near_columns(t)
                hidden2(t - 1)

            hidden1(T - 1)
            dve.wait_ge(last_h2_done, 2)
            dve.wait_ge(y_done, T - 2)
            dve.tensor_scalar(h2[:, (T - 1) % 2, 1, :], last_h2_ps[1], b2_sb[:, 1:2], 0.0,
                              ALU.add, ALU.max).then_inc(last_h2_ready[1], 1)
            output(T - 2)
            output(T - 1)

        @block.scalar
        def _(act):
            def split_high(n):
                act.wait_ge(tab_in[n % NTAB], 32 * (n // NTAB + 1))
                if n >= 3:
                    act.wait_ge(onehot_used, before[n - 2])
                w = chunks[n] * D
                act.copy(tab_hi[:, n % 3, 0:w], tab[:, n % NTAB, 0:w]).then_inc(hi_ready, 1)

            act.wait_ge(ident_in_s, 16)
            act.copy(spread[:, :], ident[0:H, 0:H]).then_inc(ids_cast, 1)

            def onehots(n):
                if n == 0:
                    act.wait_ge(hot_row_in_s, 16)
                act.wait_ge(ids_all_in[n % NTAB], 16 * (n // NTAB + 1))
                j = n
                some = by_scalar[j][1]
                for k, c in enumerate(some):
                    if j >= 1:
                        act.wait_ge(onehot_s_ready, j)
                    act.activation(distance[:, k, :], ids_all[:, n % NTAB, :], ACT.Abs,
                                   bias=hot_row[0:R, 1, int(chunks[n] != MAXC), c:c + 1]).then_inc(distance_ready, 1)
                act.wait_ge(distance_ready, GROUP * (j + 1))
                if j >= NGROUP:
                    act.wait_ge(onehot_used, used_up(by_scalar, j - NGROUP))
                act.activation(onehot_s[:, j % NGROUP, :, :], distance[:, :, :], ACT.Relu,
                               bias=1.0, scale=-1.0).then_inc(onehot_s_ready, 1)

            def move_banks(banks):
                for n in banks:
                    if n % 2 == 1:
                        evacuate(act.copy, act, n).then_inc(tp_copied_s, 1)

            split_high(0)
            onehots(0)
            if H > 1:
                split_high(1)
            for n in range(H):
                if n + 1 < H:
                    onehots(n + 1)
                if n + 2 < H:
                    split_high(n + 2)
                move_banks(early(n))
                act.wait_ge(onehot_used, before[n + 1])
                rows_t = hot_ps[n % 2][:, :].rearrange("d (t b) -> d t b", t=T)
                act.copy(xt[:, :, :, G + n], rows_t).then_inc(hot_copied, 1)

            def all_far_columns(t):
                if t == 0:
                    act.wait_ge(z_zeroed, 1)
                for s in range(PACK):
                    act.wait_ge(gram_ready, 2 * t + s // (PACK // 2) + 1)
                    for g in range(PACK):
                        cells, columns, _ = pack_operands(t, s, g, HF, SLOTS)
                        last = act.copy(cells, columns)
                    last.then_inc(far_columns, 1)

            def hidden1(t):
                if t == 0:
                    act.wait_ge(small_in, 48)
                act.wait_ge(h1_done, 2 * t + 1)
                if t >= 2:
                    act.wait_ge(h2_done, t - 1)
                for k in range(HM):
                    last = act.activation(h1[:, t % 2, k, :], h1_ps[0][:, k, :], ACT.Relu, bias=b1_sb[:, k:k + 1])
                last.then_inc(h1_s_ready, 1)

            for t in range(T):
                if t == 0:
                    move_banks(ahead(t, range(2)))
                    all_far_columns(t)
                    move_banks(ahead(t, [2]))
                    continue
                move_banks(ahead(t, range(HM)))
                hidden1(t - 1)
                move_banks(ahead(t, range(HM, M1 + 1)))
                all_far_columns(t)

            hidden1(T - 1)
            act.wait_ge(last_h2_done, 1)
            act.wait_ge(y_done, T - 2)
            act.activation(h2[:, (T - 1) % 2, 0, :], last_h2_ps[0], ACT.Relu,
                           bias=b2_sb[:, 0:1]).then_inc(last_h2_ready[0], 1)


def kernel(**inputs):
    import numpy as np
    import concourse.bacc as bacc
    from concourse.bass_utils import run_bass_kernel_spmd

    nc = bacc.Bacc("TRN2", target_bir_lowering=False, num_devices=1)
    w1 = np.asarray(inputs["W_top1"])
    n1 = w1.shape[1]
    tables = [np.asarray(inputs[f"tbl_{f}"]) for f in range(F)]
    hot = sorted(sorted(range(F), key=lambda f: (tables[f].shape[0], f))[:HOT])
    gathered = [f for f in range(F) if f not in hot]
    order = gathered + hot
    w_inter = np.zeros((P, NC, n1), w1.dtype)
    mask = np.zeros((P, NC), np.int32)
    for k in range(SLOTS):
        for r in range(F):
            far = k <= r < k + HF
            mask[Q * (k % PACK) + r, k // PACK] = not far
            if far or (k < SLOTS - 1 and r != k + HF):
                i, j = order[r], order[k + HF if far else k]
                i, j = max(i, j), min(i, j)
                w_inter[Q * (k % PACK) + r, k // PACK] = w1[D + i * (i - 1) // 2 + j]
    c, p = np.arange(MAXC), np.arange(P)[:, None]
    hot_row = np.stack([p * MAXC + c, p * 8 + c], axis=1)
    hot_row = np.stack([hot_row, -hot_row], axis=1).astype(np.float32)
    w_bottom = np.ascontiguousarray(np.stack([w1[:D], w1[-D:]], axis=1))

    def columns(a):
        a = np.asarray(a)
        return np.ascontiguousarray(a.reshape((a.shape[0] // P, P) + a.shape[1:]).swapaxes(0, 1))

    arrays = {
        "bottom": np.asarray(inputs["r_bottom_mlp_out"]), "ids": np.asarray(inputs["ids"]),
        "w_bottom": w_bottom, "w_inter": w_inter, "b1": columns(inputs["b_top1"]),
        "w2": columns(inputs["W_top2"]), "b2": columns(inputs["b_top2"]),
        "w3": columns(np.asarray(inputs["W_top3"])[:, 0]), "ident": np.eye(P, dtype=np.float32),
    }
    arrays["ids_hot"] = np.ascontiguousarray(arrays["ids"].T[hot])
    arrays["hot_row"] = hot_row
    arrays["mask"] = mask
    for f in range(F):
        arrays[f"tbl_{f}"] = tables[f]
    ap = {k: nc.dram_tensor(k + "_dram", a.shape, mybir.dt.from_np(a.dtype), kind="ExternalInput").ap() for k, a in arrays.items()}
    out = nc.dram_tensor("y_dram", (arrays["bottom"].shape[0], 1), F32, kind="ExternalOutput").ap()
    build_tower(nc, ap["bottom"], ap["ids"], ap["ids_hot"], [ap[f"tbl_{f}"] for f in range(F)], gathered, hot,
                ap["w_bottom"], ap["w_inter"],
                ap["b1"], ap["w2"], ap["b2"], ap["w3"], ap["ident"], ap["hot_row"], ap["mask"], out)
    r = run_bass_kernel_spmd(nc, [{k + "_dram": a for k, a in arrays.items()}], core_ids=[0])
    return r.results[0]["y_dram"]
```
